# Optimizing a Trainium2 kernel written in Bass

```python
import numpy as np
import jax
import jax.numpy as jnp

def _softmax(x, axis=-1):
    return jax.nn.softmax(x, axis=axis)

def _gelu(x):
    return jax.nn.gelu(x, approximate=True)

def _silu(x):
    return jax.nn.silu(x)

def _sigmoid(x):
    return jax.nn.sigmoid(x)

def _layernorm(x, axis=-1, eps=1e-05):
    m = jnp.mean(x, axis=axis, keepdims=True)
    v = jnp.var(x, axis=axis, keepdims=True)
    return (x - m) / jnp.sqrt(v + eps)

def _scatter_add(tgt, idx, src, axis=0):
    return tgt.at[idx].add(src)

def _segment_sum(src, seg, n):
    return jax.ops.segment_sum(src, seg, n)
kernel_name = 'mk_flamingo_gated_d1_seqx_r8_2be15c'

def setup_inputs(seed: int=0):
    np.random.seed(seed)
    _w = jnp.asarray

    def _rec_inputs():
        import jax
        import jax.numpy as jnp
        _rk = jax.random.key(seed)
        x = -0.0002928 + 1 * jax.random.normal(jax.random.fold_in(_rk, 1), (8, 128, 128), jnp.float32)
        _lenS = 128 - jax.random.randint(jax.random.fold_in(_rk, 7), (8,), 0, max(1, 128 // 4) + 1, jnp.int32)
        _lenS2 = 128 - jax.random.randint(jax.random.fold_in(_rk, 8), (8,), 0, max(1, 128 // 4) + 1, jnp.int32)
        _ctx_1024P = jax.random.normal(jax.random.fold_in(_rk, 11), (8, 16, 128), jnp.float32)
        _ctx_1024c = jax.random.dirichlet(jax.random.fold_in(_rk, 511), 0.3 * jnp.ones((16,), jnp.float32), (8, 128))
        _ctx_1024t = jnp.einsum('bsk,bkd->bsd', _ctx_1024c, _ctx_1024P)
        _ctx_1024t = _ctx_1024t * jax.lax.rsqrt(jnp.mean(jnp.square(_ctx_1024t)) + 1e-12) * 0.953939
        ctx_1024 = -1.39393e-06 + 0.999914 * (_ctx_1024t + 0.3 * jax.random.normal(jax.random.fold_in(_rk, 611), (8, 128, 128), jnp.float32))
        _g = jax.random.normal(jax.random.fold_in(_rk, 9001), (2, 1), jnp.float32)
        _g = jnp.sign(_g) * jnp.maximum(jnp.abs(_g), 1.0) + (_g == 0) * 1.0
        g_xattn = _g[0]
        g_ffn = _g[1]
        return (x, ctx_1024, g_xattn, g_ffn)
    x, ctx_1024, g_xattn, g_ffn = _rec_inputs()

    def _L0_xattn_setup():
        import jax, jax.numpy as jnp
        import numpy as np
        MODEL_DIM = 128
        NUM_HEADS = 16
        HEAD_DIM = MODEL_DIM // NUM_HEADS
        SCALE = HEAD_DIM ** (-0.5)
        key = jax.random.key(seed)
        ks = jax.random.split(key, 8)
        B, LQ, LC = (2, 256, 256)
        std = MODEL_DIM ** (-0.5)
        return {'query': jax.random.normal(ks[0], (B, LQ, MODEL_DIM), jnp.float32), 'context': jax.random.normal(ks[1], (B, LC, MODEL_DIM), jnp.float32), 'Wq': jax.random.normal(ks[2], (MODEL_DIM, MODEL_DIM), jnp.float32) * std, 'bq': jnp.zeros((MODEL_DIM,), jnp.float32), 'Wkv': jax.random.normal(ks[3], (MODEL_DIM, 2 * MODEL_DIM), jnp.float32) * std, 'bkv': jnp.zeros((2 * MODEL_DIM,), jnp.float32), 'Wout': jax.random.normal(ks[4], (MODEL_DIM, MODEL_DIM), jnp.float32) * std, 'bout': jnp.zeros((MODEL_DIM,), jnp.float32)}
    _L0_xattn_all = _L0_xattn_setup()
    _L0_xattn_in = {k: v for k, v in _L0_xattn_all.items() if k in ('Wq', 'bq', 'Wkv', 'bkv', 'Wout', 'bout')}
    del _L0_xattn_all

    def _L0_ffn_setup():
        import jax, jax.numpy as jnp
        import numpy as np
        TOP_K = 2
        EPS = 1e-09
        key = jax.random.key(seed)
        ks = jax.random.split(key, 6)
        B, T, D, H, E = (4, 256, 128, 256, 8)
        x = jax.random.normal(ks[0], (B, T, D), dtype=jnp.float32)
        Wg = jax.random.normal(ks[1], (E, D), dtype=jnp.float32) * 0.02
        W1 = jax.random.normal(ks[2], (E, 2 * H, D), dtype=jnp.float32) * 0.02
        b1 = jax.random.normal(ks[3], (E, 2 * H), dtype=jnp.float32) * 0.02
        Wo = jax.random.normal(ks[4], (D, H), dtype=jnp.float32) * 0.02
        bo = jax.random.normal(ks[5], (D,), dtype=jnp.float32) * 0.02
        return {'x': x, 'Wg': Wg, 'W1': W1, 'b1': b1, 'Wo': Wo, 'bo': bo}
    _L0_ffn_all = _L0_ffn_setup()
    _L0_ffn_in = {k: v for k, v in _L0_ffn_all.items() if k in ('Wg', 'W1', 'b1', 'Wo', 'bo')}
    del _L0_ffn_all
    return {'x': x, 'ctx_1024': ctx_1024, 'g_xattn': g_xattn, 'g_ffn': g_ffn, 'L0_xattn_Wq': _L0_xattn_in['Wq'], 'L0_xattn_bq': _L0_xattn_in['bq'], 'L0_xattn_Wkv': _L0_xattn_in['Wkv'], 'L0_xattn_bkv': _L0_xattn_in['bkv'], 'L0_xattn_Wout': _L0_xattn_in['Wout'], 'L0_xattn_bout': _L0_xattn_in['bout'], 'L0_ffn_Wg': _L0_ffn_in['Wg'], 'L0_ffn_W1': _L0_ffn_in['W1'], 'L0_ffn_b1': _L0_ffn_in['b1'], 'L0_ffn_Wo': _L0_ffn_in['Wo'], 'L0_ffn_bo': _L0_ffn_in['bo']}

def reference(x, ctx_1024, g_xattn, g_ffn, L0_xattn_Wq, L0_xattn_bq, L0_xattn_Wkv, L0_xattn_bkv, L0_xattn_Wout, L0_xattn_bout, L0_ffn_Wg, L0_ffn_W1, L0_ffn_b1, L0_ffn_Wo, L0_ffn_bo):
    import jax
    import jax.numpy as jnp

    def _L0_xattn_ref(query, context, Wq, bq, Wkv, bkv, Wout, bout):
        import jax, jax.numpy as jnp
        import numpy as np
        MODEL_DIM = 128
        NUM_HEADS = 16
        HEAD_DIM = MODEL_DIM // NUM_HEADS
        SCALE = HEAD_DIM ** (-0.5)
        B, LQ, _ = query.shape
        LC = context.shape[1]
        H, D = (NUM_HEADS, HEAD_DIM)
        q = query @ Wq + bq
        kv = context @ Wkv + bkv
        kv = kv.reshape(B, LC, H, D, 2)
        k = jnp.transpose(kv[..., 0], (0, 2, 1, 3))
        v = jnp.transpose(kv[..., 1], (0, 2, 1, 3))
        q = jnp.transpose(q.reshape(B, LQ, H, D), (0, 2, 1, 3))
        scores = jnp.einsum('bhid,bhjd->bhij', q, k) * SCALE
        attn = jax.nn.softmax(scores, axis=-1)
        out = jnp.einsum('bhij,bhjd->bhid', attn, v)
        out = jnp.transpose(out, (0, 2, 1, 3)).reshape(B, LQ, H * D)
        return out @ Wout + bout

    def _L0_ffn_ref(x, Wg, W1, b1, Wo, bo):
        import jax, jax.numpy as jnp
        import numpy as np
        TOP_K = 2
        EPS = 1e-09
        E = Wg.shape[0]
        gate_logits = jnp.einsum('btd,ed->bte', x, Wg)
        gate_scores = jax.nn.softmax(gate_logits, axis=-1)
        topk_val, topk_idx = jax.lax.top_k(gate_scores, TOP_K)
        topk_val = topk_val / (topk_val.sum(axis=-1, keepdims=True) + EPS)
        comb = (jax.nn.one_hot(topk_idx, E, dtype=x.dtype) * topk_val[..., None]).sum(axis=-2)
        out = jnp.zeros_like(x)
        for e in range(E):
            h = jnp.einsum('btd,hd->bth', x, W1[e]) + b1[e]
            a, b = jnp.split(h, 2, axis=-1)
            g = a * jax.nn.sigmoid(b)
            eo = jnp.einsum('bth,dh->btd', g, Wo) + bo
            out = out + eo * comb[..., e:e + 1]
        return out
    x = x + jnp.tanh(g_xattn[0]) * _L0_xattn_ref(_layernorm(x, axis=-1), ctx_1024, L0_xattn_Wq, L0_xattn_bq, L0_xattn_Wkv, L0_xattn_bkv, L0_xattn_Wout, L0_xattn_bout)
    x = x + jnp.tanh(g_ffn[0]) * _L0_ffn_ref(_layernorm(x, axis=-1), L0_ffn_Wg, L0_ffn_W1, L0_ffn_b1, L0_ffn_Wo, L0_ffn_bo)
    return x

_drawn_inputs = setup_inputs


def setup_inputs(seed=0):
    import zlib

    import numpy as np

    out = dict(_drawn_inputs(seed))
    spreads = {'L0_xattn_bq': (0.0, 0.456), 'L0_xattn_bkv': (0.0, 0.1), 'L0_xattn_bout': (0.0, 0.1)}
    factors = {'L0_ffn_Wg': 2.881, 'L0_ffn_b1': 26.724, 'L0_ffn_bo': 2.779}
    for name, (base, spread) in spreads.items():
        noise = np.random.default_rng([zlib.crc32(name.encode()), seed]).standard_normal(out[name].shape)
        drawn = base * np.exp(spread * noise) if base else spread * noise
        out[name] = jnp.asarray(drawn.astype(out[name].dtype))
    for name, factor in factors.items():
        out[name] = (out[name] * factor).astype(out[name].dtype)
    return out
```

```python
import concourse.bass as bass
from concourse import mybir
from contextlib import ExitStack


def flamingo_gated_block(nc, x, ctx_in, g_xattn, g_ffn, Wq, bq, Wkv, bkv, Wout, bout, Wg, W1, b1, Wo, bo, out):
    fp32, fp32r, u32 = mybir.dt.float32, mybir.dt.float32r, mybir.dt.uint32
    ALU, ACT, AX = mybir.AluOpType, mybir.ActivationFunctionType, mybir.AxisListType

    T, P, D = x.shape
    NH = 16
    HD = D // NH
    NG = 4
    HG = NH // NG
    GP = P // NG
    SCALE = float(HD) ** -0.5
    NE, H2, _ = W1.shape
    NC = H2 // P
    HH = H2 // 2
    PH = HH // NC
    LN_EPS, TOP_EPS = 1e-5, 1e-9
    RB = 4
    PAIRS = NE // 2

    es = ExitStack()
    with es:
        def sb(name, shape, dt=fp32):
            return es.enter_context(nc.sbuf_tensor(name, shape, dt))

        def sem(name):
            return es.enter_context(nc.semaphore(name))

        xs = sb("xs", [P, T, D])
        cs = sb("cs", [P, T, D])
        wq = sb("wq", [D, D])
        wkv = sb("wkv", [D, 2 * D])
        wout = sb("wout", [D, D])
        wo = sb("wo", [D, HH])
        wg = sb("wg", [NE, D])
        w1 = sb("w1", [P, NE, NC * D])
        b1s = sb("b1s", [P, NE, NC])
        bqk = sb("bqk", [D, 3])
        bvb = sb("bvb", [P, 2 * D])
        boutb = sb("boutb", [P, D])
        bob = sb("bob", [P, D])
        gates = sb("gates", [P, 2])
        ident = sb("ident", [P, P])
        head_mask = sb("head_mask", [P, HG])
        row_mask = sb("row_mask", [P, HG])
        ones_r = sb("ones_r", [P, P], fp32r)
        ones_f = sb("ones_f", [P, P])
        half_pow = sb("half_pow", [P, T])
        iota8 = sb("iota8", [P, NE])
        tanh_g = sb("tanh_g", [P, 2])
        wqk = sb("wqk", [D, 2, D])
        wv = sb("wv", [D, D])
        wout_t = sb("wout_t", [D, D])
        wo_t = sb("wo_t", [D, HH])
        woT = sb("woT", [P, 2, D])
        wgT = sb("wgT", [D, NE])
        bob_t = sb("bob_t", [P, D])
        stats = sb("stats", [P, T, 6])
        mv = sb("mv", [P, T, 2])
        var_eps = sb("var_eps", [P, T])
        rstd = sb("rstd", [P, T])
        xn = sb("xn", [P, 2, D])
        xcT = sb("xcT", [D, 2, 2 * P])
        qk = sb("qk", [D, 2, 2, P])
        qk_hi = sb("qk_hi", [D, 3, 2, P], fp32r)
        qk_lo = sb("qk_lo", [D, 3, 2, P], fp32r)
        q_hi_m = sb("q_hi_m", [D, 3, HG, P], fp32r)
        q_lo_m = sb("q_lo_m", [D, 3, HG, P], fp32r)
        k_hi_m = sb("k_hi_m", [D, 2, HG, P], fp32r)
        v_pad = sb("v_pad", [P, 3, NH, GP])
        neg_max = sb("neg_max", [P, 2, P])
        max_m = sb("max_m", [P, 2, HG, P], fp32r)
        probs = sb("probs", [P, 2, NG, HG * P])
        o_sb = sb("o_sb", [P, 2, NG, P])
        rden = sb("rden", [P, NH])
        att = sb("att", [P, 2, D])
        attT = sb("attT", [D, 2, P])
        x1 = sb("x1", [P, T, D])
        stats2 = sb("stats2", [P, 2, 6])
        mv2 = sb("mv2", [P, 2, 2])
        var2 = sb("var2", [P, 2])
        rstd2 = sb("rstd2", [P, 2])
        xn2 = sb("xn2", [P, 2, D])
        xn2T = sb("xn2T", [D, 2, P])
        x_hi = sb("x_hi", [D, T, P], fp32r)
        x_lo = sb("x_lo", [D, T, P], fp32r)
        lg = sb("lg", [P, T, NE])
        lmax = sb("lmax", [P, RB])
        lsub = sb("lsub", [P, RB, NE])
        pe8 = sb("pe8", [P, RB, NE])
        psum8 = sb("psum8", [P, RB])
        prec8 = sb("prec8", [P, RB])
        pr8 = sb("pr8", [P, RB, NE])
        top8 = sb("top8", [P, RB, 8])
        idx8 = sb("idx8", [P, RB, 8], u32)
        idxf = sb("idxf", [P, RB, 2])
        s2 = sb("s2", [P, RB])
        r2 = sb("r2", [P, RB])
        w2 = sb("w2", [P, RB, 2])
        eq8 = sb("eq8", [P, 2, RB, NE])
        comb = sb("comb", [P, T, NE])
        scomb = sb("scomb", [P, T])
        wsum = sb("wsum", [P, NE, NC])
        w1b = sb("w1b", [P, NE, NC])
        w1a = sb("w1a", [P, 2, NC * D])
        w_hi = sb("w_hi", [D, NE, H2], fp32r)
        w_lo = sb("w_lo", [D, NE, H2], fp32r)
        sig = sb("sig", [P, 3, 2, HH])
        gl = sb("gl", [P, 4, HH])
        gacc = sb("gacc", [P, 2, HH])
        gsum = sb("gsum", [P, 2, HH])
        gb = sb("gb", [P, HH])
        gT = sb("gT", [P, 2, 2, P])
        y = sb("y", [P, 2, D])

        ps = es.enter_context(nc.psum_tensor("ps", [P, 8, 512], fp32))
        MXB, SCB, PVB, AB, WB, OB = 0, 2, 4, 5, 6, 7

        d_x = [sem(f"d_x{n}") for n in range(2)]
        d_c = [sem(f"d_c{n}") for n in range(2)]
        d_w1 = [sem(f"d_w1_{n}") for n in range(4)]
        d_out = [sem(f"d_out{n}") for n in range(2)]
        d_g, d_wq, d_wkv, d_bqk, d_bv, d_bout, d_wout, d_wo, d_wg, d_bo, d_b1 = [
            sem(n) for n in ("d_g", "d_wq", "d_wkv", "d_bqk", "d_bv", "d_bout", "d_wout", "d_wo", "d_wg", "d_bo",
                             "d_b1")]
        (s_setup, s_AT, s_AP, s_MX, s_mT, s_SC, s_PV, s_OT, s_aT, s_OP, s_XT, s_RT, s_WT, s_FF, s_GT, s_WO) = [
            sem(n) for n in ("s_setup", "s_AT", "s_AP", "s_MX", "s_mT", "s_SC", "s_PV", "s_OT", "s_aT", "s_OP",
                             "s_XT", "s_RT", "s_WT", "s_FF", "s_GT", "s_WO")]
        (a_tanh, a_setup, a_xc, a_hi, a_exp, a_o, a_aT, a_xT, a_lg, a_re, a_wh, a_sig, a_gT) = [
            sem(n) for n in ("a_tanh", "a_setup", "a_xc", "a_hi", "a_exp", "a_o", "a_aT", "a_xT", "a_lg", "a_re",
                             "a_wh", "a_sig", "a_gT")]
        (v_chain, v_masks, v_wqk, v_var, v_xres, v_xn, v_qk, v_v, v_lo, v_max, v_mm, v_at, v_x1, v_var2, v_xn2,
         v_x2, v_sub, v_comb, v_b1, v_wo, v_wl, v_woT, v_ones, v_g, v_gs, v_y) = [
            sem(n) for n in ("v_chain", "v_masks", "v_wqk", "v_var", "v_xres", "v_xn", "v_qk", "v_v", "v_lo",
                             "v_max", "v_mm", "v_at", "v_x1", "v_var2", "v_xn2", "v_x2", "v_sub", "v_comb",
                             "v_b1", "v_wo", "v_wl", "v_woT", "v_ones", "v_g", "v_gs", "v_y")]
        (p_zero, p_ident, p_const, p_rstd, p_km, p_qh, p_ql, p_rstd2, p_wa, p_acc) = [
            sem(n) for n in ("p_zero", "p_ident", "p_const", "p_rstd", "p_km", "p_qh", "p_ql", "p_rstd2", "p_wa",
                             "p_acc")]

        block = es.enter_context(nc.Block())

        def bc(ap, n):
            return ap.unsqueeze(2).to_broadcast([ap.shape[0], ap.shape[1], n])

        def rep(ap, n):
            return ap.unsqueeze(1).to_broadcast([ap.shape[0], n, ap.shape[1]])

        iters = range(-2, T + 2)

        def on(t):
            return 0 <= t < T

        @block.sync
        def _(sp):
            xt, ct, h = x.rearrange("t p d -> p t d"), ctx_in.rearrange("t p d -> p t d"), T // 2
            w1t = W1.rearrange("e (p c) d -> p e (c d)", c=NC)
            sp.dma_start(xs[:, 0:h], xt[:, 0:h]).then_inc(d_x[0], 16)
            sp.dma_start(cs[:, 0:h], ct[:, 0:h]).then_inc(d_c[0], 16)
            sp.dma_start(wq[:, :], Wq).then_inc(d_wq, 16)
            sp.dma_start(xs[:, h:T], xt[:, h:T]).then_inc(d_x[1], 16)
            sp.dma_start(cs[:, h:T], ct[:, h:T]).then_inc(d_c[1], 16)
            for n in range(4):
                sp.dma_start(w1[:, 2 * n:2 * n + 2, :], w1t[:, 2 * n:2 * n + 2, :]).then_inc(d_w1[n], 16)
            for t in range(T):
                sp.wait_ge(v_y, t + 1)
                sp.dma_start(out[t], y[:, t % 2, :]).then_inc(d_out[t % 2], 16)
            for n in range(2):
                sp.wait_ge(d_out[n], 16 * (T // 2))

        @block.gpsimd
        def _(pool):
            nc.gpsimd.memset(ident[:, :], 0.0).then_inc(p_zero, 1)
            pool.wait_ge(p_zero, 1)
            nc.gpsimd.affine_select(out=ident[:, :], in_=ident[:, :], compare_op=ALU.not_equal, fill=1.0, base=0,
                                    pattern=[[-1, P]], channel_multiplier=1).then_inc(p_ident, 1)
            nc.gpsimd.memset(half_pow[:, :], -0.5).then_inc(p_const, 1)
            for e in range(NE):
                last = nc.gpsimd.memset(iota8[:, e:e + 1], float(e))
            last.then_inc(p_const, 1)
            nc.gpsimd.memset(v_pad[:, :, :, :], 0.0).then_inc(p_const, 1)
            nc.gpsimd.memset(neg_max[:, :, :], 0.0).then_inc(p_const, 1)
            pool.wait_ge(p_const, 4)
            nc.gpsimd.memset(v_pad[:, :, :, HD:HD + 1], 1.0).then_inc(p_const, 1)
            pool.wait_ge(v_var, 1)
            nc.gpsimd.tensor_tensor(rstd[:, :], var_eps[:, :], half_pow[:, :], ALU.pow).then_inc(p_rstd, 1)

            def biased_w1(e):
                pool.wait_ge(v_b1, e + 1)
                if e >= 2:
                    pool.wait_ge(s_WT, e - 1)
                nc.gpsimd.tensor_tensor(w1a[:, e % 2, :].rearrange("p (c d) -> p c d", c=NC),
                                        w1[:, e, :].rearrange("p (c d) -> p c d", c=NC),
                                        bc(w1b[:, e, :], D), ALU.add).then_inc(p_wa, 1)

            def masked(t):
                hm = bc(head_mask[:, :], P)
                if t == 0:
                    pool.wait_ge(v_masks, 1)
                pool.wait_ge(a_hi, t + 1)
                if t >= 2:
                    pool.wait_ge(s_MX, NG * (t - 1))
                nc.gpsimd.tensor_tensor(k_hi_m[:, t % 2], rep(qk_hi[:, t % 3, 1, :].bitcast(fp32), HG), hm,
                                        ALU.mult).then_inc(p_km, 1)
                if t >= 3:
                    pool.wait_ge(s_SC, NG * (t - 2))
                nc.gpsimd.tensor_tensor(q_hi_m[:, t % 3], rep(qk_hi[:, t % 3, 0, :].bitcast(fp32), HG), hm,
                                        ALU.mult).then_inc(p_qh, 1)
                pool.wait_ge(v_lo, t + 1)
                nc.gpsimd.tensor_tensor(q_lo_m[:, t % 3], rep(qk_lo[:, t % 3, 0, :].bitcast(fp32), HG), hm,
                                        ALU.mult).then_inc(p_ql, 1)

            biased_w1(0)
            for i in iters:
                if on(i + 3):
                    biased_w1(i + 3)
                if on(i + 2):
                    masked(i + 2)
                if on(i - 1):
                    t = i - 1
                    pool.wait_ge(v_var2, t + 1)
                    nc.gpsimd.tensor_tensor(rstd2[:, t % 2:t % 2 + 1], var2[:, t % 2:t % 2 + 1],
                                            half_pow[:, 0:1], ALU.pow).then_inc(p_rstd2, 1)
            for t in range(T):
                for e in range(1, NE - 2):
                    pool.wait_ge(v_g, NE * t + e + 1)
                    if e > 1:
                        pool.wait_ge(p_acc, (NE - 3) * t + e - 1)
                    nc.gpsimd.tensor_tensor(gacc[:, t % 2, :], gacc[:, t % 2, :], gl[:, e % 4, :],
                                            ALU.add).then_inc(p_acc, 1)

        @block.scalar
        def _(act):
            act.dma_start(gates[:, 0:1], g_xattn.partition_broadcast(P)).then_inc(d_g, 16)
            act.dma_start(gates[:, 1:2], g_ffn.partition_broadcast(P)).then_inc(d_g, 16)
            act.dma_start(wkv[:, :], Wkv).then_inc(d_wkv, 16)
            act.dma_start(bqk[:, 0:1], bq.unsqueeze(1)).then_inc(d_bqk, 16)
            act.dma_start(bqk[:, 1:3], bkv.rearrange("(d two) -> d two", two=2)).then_inc(d_bqk, 16)
            act.dma_start(bvb[:, :], bkv.partition_broadcast(P)).then_inc(d_bv, 16)
            act.dma_start(boutb[:, :], bout.partition_broadcast(P)).then_inc(d_bout, 16)
            act.dma_start(wout[:, :], Wout).then_inc(d_wout, 16)
            act.dma_start(b1s[:, :, :], b1.rearrange("e (p c) -> p e c", c=NC)).then_inc(d_b1, 16)
            act.dma_start(wo[:, :], Wo).then_inc(d_wo, 16)
            act.dma_start(wg[:, :], Wg).then_inc(d_wg, 16)
            act.dma_start(bob[:, :], bo.partition_broadcast(P)).then_inc(d_bo, 16)
            act.wait_ge(d_g, 32)
            nc.scalar.activation(tanh_g[:, :], gates[:, :], ACT.Tanh).then_inc(a_tanh, 1)

            def exp(t, g):
                act.wait_ge(s_SC, NG * t + g + 1)
                if t >= 2:
                    act.wait_ge(s_PV, NG * (t - 2) + g + 1)
                nc.scalar.activation(probs[:, t % 2, g, :], ps[:, SCB + g % 2, :], ACT.Exp).then_inc(a_exp, 1)

            for i in iters:
                if on(i + 2):
                    t = i + 2
                    act.wait_ge(s_AT, t + 1)
                    if t >= 2:
                        act.wait_ge(s_AP, t - 1)
                    nc.scalar.copy(xcT[:, t % 2, :], ps[:, AB, 0:2 * P]).then_inc(a_xc, 1)
                if on(i):
                    exp(i, 0)
                    exp(i, 1)
                if on(i + 2):
                    act.wait_ge(v_qk, t + 1)
                    if t >= 3:
                        act.wait_ge(s_SC, NG * (t - 2))
                        act.wait_ge(p_ql, t - 2)
                    nc.scalar.copy(qk_hi[:, t % 3, :, :], qk[:, t % 2, :, :]).then_inc(a_hi, 1)
                if on(i - 1):
                    t = i - 1
                    act.wait_ge(s_aT, t + 1)
                    if t >= 2:
                        act.wait_ge(s_OP, t - 1)
                    nc.scalar.copy(attT[:, t % 2, :], ps[:, OB, 0:P]).then_inc(a_aT, 1)
                if on(i):
                    exp(i, 2)
                if on(i + 2):
                    e = i + 2
                    act.wait_ge(s_WT, e + 1)
                    nc.scalar.copy(w_hi[:, e, :], ps[:, WB, :]).then_inc(a_wh, 1)
                if on(i):
                    exp(i, 3)
                if on(i - 2):
                    t = i - 2
                    act.wait_ge(s_XT, t + 1)
                    if t >= 2:
                        act.wait_ge(s_RT, t - 1)
                        act.wait_ge(v_x2, t - 1)
                    nc.scalar.copy(xn2T[:, t % 2, :], ps[:, OB, 0:P]).then_inc(a_xT, 1)
                    act.wait_ge(s_RT, t + 1)
                    nc.scalar.copy(lg[:, t, :], ps[:, OB, 0:NE]).then_inc(a_lg, 1)
                    if t % RB == RB - 1:
                        b = t // RB
                        act.wait_ge(v_sub, b + 1)
                        nc.scalar.activation(pe8[:, :, :], lsub[:, :, :], ACT.Exp).then_inc(a_re, 1)
                if on(i):
                    act.wait_ge(s_PV, NG * (i + 1))
                    if i >= 2:
                        act.wait_ge(s_OT, i - 1)
                    nc.scalar.copy(o_sb[:, i % 2, :, :], ps[:, PVB, :]).then_inc(a_o, 1)

            def hidden_out(t):
                act.wait_ge(s_GT, t + 1)
                if t >= 2:
                    act.wait_ge(s_WO, t - 1)
                nc.scalar.copy(gT[:, t % 2, :, :], ps[:, 6, 0:2 * P]).then_inc(a_gT, 1)

            for t in range(T):
                for j in range(PAIRS):
                    n = PAIRS * t + j
                    act.wait_ge(s_FF, n + 1)
                    if n >= 3:
                        act.wait_ge(v_g, 2 * (n - 2))
                    b = 2 * (n % 3)
                    nc.scalar.activation(
                        sig[:, n % 3, :, :].rearrange("p e (c h) -> p e c h", c=NC),
                        ps[:, b:b + 2, :].rearrange("p e (c h) -> p e c h", c=NC)[:, :, :, PH:P],
                        ACT.Sigmoid).then_inc(a_sig, 1)
                    if j == 1 and t >= 1:
                        hidden_out(t - 1)
            hidden_out(T - 1)

        @block.vector
        def _(dve):
            chain = [0]

            def link(ins):
                chain[0] += 1
                ins.then_inc(v_chain, 1)
                dve.wait_ge(v_chain, chain[0])

            for t in range(T):
                if t % (T // 2) == 0:
                    dve.wait_ge(d_x[t // (T // 2)], 16)
                last = nc.vector.bn_stats(stats[:, t, :], xs[:, t, :])
            link(last)
            for t in range(T):
                last = nc.vector.bn_aggr(mv[:, t, :], stats[:, t, :])
            link(last)
            nc.vector.tensor_scalar(var_eps[:, :], mv[:, :, 1], LN_EPS, None, ALU.add).then_inc(v_var, 1)
            dve.wait_ge(p_ident, 1)
            nc.vector.tensor_reduce(head_mask[:, :], ident[:, :].rearrange("p (g r d) -> p r g d", g=NG, r=HG),
                                    AX.XY, ALU.add)
            nc.vector.tensor_reduce(row_mask[:, :], ident[:, :].rearrange("p (g c) -> p c g", g=NG)[:, 0:HG, :],
                                    AX.X, ALU.add).then_inc(v_masks, 1)
            nc.vector.memset(ones_f[:, :], 1.0).then_inc(v_ones, 1)
            dve.wait_ge(v_ones, 1)
            nc.vector.tensor_copy(ones_r[:, :], ones_f[:, :]).then_inc(v_ones, 1)
            dve.wait_ge(d_wq, 16)
            nc.vector.tensor_scalar(wqk[:, 0, :], wq[:, :], SCALE, None, ALU.mult)
            dve.wait_ge(d_wkv, 16)
            kv = wkv[:, :].rearrange("p (d two) -> p two d", two=2)
            nc.vector.tensor_copy(wqk[:, 1, :], kv[:, 0, :])
            dve.wait_ge(d_bqk, 32)
            nc.vector.tensor_scalar(bqk[:, 0:1], bqk[:, 0:1], SCALE, None, ALU.mult)
            nc.vector.tensor_copy(wv[:, :], kv[:, 1, :]).then_inc(v_wqk, 1)

            def row_sums(e):
                dve.wait_ge(d_w1[e // 2], 16)
                link(nc.vector.tensor_reduce(wsum[:, e, :], w1[:, e, :].rearrange("p (c d) -> p c d", c=NC),
                                             AX.X, ALU.add))
                if e == 0:
                    dve.wait_ge(d_b1, 16)
                link(nc.vector.tensor_tensor(w1b[:, e, :], b1s[:, e, :], wsum[:, e, :], ALU.subtract))
                nc.vector.tensor_scalar(w1b[:, e, :], w1b[:, e, :], 1.0 / D, None, ALU.mult).then_inc(v_b1, 1)

            def normalized(t):
                if t == 0:
                    dve.wait_ge(p_rstd, 1)
                if t >= 2:
                    dve.wait_ge(s_AT, t - 1)
                nc.vector.tensor_scalar(xn[:, t % 2, :], xs[:, t, :], mv[:, t, 0:1], rstd[:, t:t + 1],
                                        ALU.subtract, ALU.mult).then_inc(v_xn, 1)

            def maxima(t, g):
                dve.wait_ge(s_MX, NG * t + g + 1)
                if g == 0 and t >= 2:
                    dve.wait_ge(s_mT, t - 1)
                if g == 0 and t == 0:
                    dve.wait_ge(p_const, 4)
                nc.vector.tensor_reduce(neg_max[:, t % 2, GP * g:GP * g + HG],
                                        ps[:, MXB + g % 2, :].rearrange("p (r j) -> p r j", r=HG),
                                        AX.X, ALU.max, negate=True).then_inc(v_max, 1)

            def router(b):
                t0 = RB * b
                L = lg[:, t0:t0 + RB, :]
                dve.wait_ge(a_lg, t0 + RB)
                link(nc.vector.tensor_reduce(lmax[:, :], L, AX.X, ALU.max))
                if b:
                    dve.wait_ge(a_re, b)
                nc.vector.tensor_tensor(lsub[:, :, :], L, bc(lmax[:, :], NE), ALU.subtract).then_inc(v_sub, 1)
                dve.wait_ge(a_re, b + 1)
                link(nc.vector.tensor_reduce(psum8[:, :], pe8[:, :, :], AX.X, ALU.add))
                link(nc.vector.reciprocal(prec8[:, :], psum8[:, :]))
                link(nc.vector.tensor_tensor(pr8[:, :, :], pe8[:, :, :], bc(prec8[:, :], NE), ALU.mult))
                for k in range(RB):
                    last = nc.vector.max(top8[:, k, :], pr8[:, k, :])
                link(last)
                for k in range(RB):
                    last = nc.vector.max_index(idx8[:, k, :], top8[:, k, :], pr8[:, k, :])
                nc.vector.tensor_tensor(s2[:, :], top8[:, :, 0], top8[:, :, 1], ALU.add)
                link(last)
                link(nc.vector.tensor_copy(idxf[:, :, :], idx8[:, :, 0:2]))
                link(nc.vector.tensor_scalar(s2[:, :], s2[:, :], TOP_EPS, None, ALU.add))
                link(nc.vector.reciprocal(r2[:, :], s2[:, :]))
                link(nc.vector.tensor_tensor(w2[:, :, :], top8[:, :, 0:2], bc(r2[:, :], 2), ALU.mult))
                for k in range(2):
                    last = nc.vector.tensor_tensor(eq8[:, k, :, :], rep(iota8[:, :], RB), bc(idxf[:, :, k], NE),
                                                   ALU.is_equal)
                link(last)
                for k in range(2):
                    last = nc.vector.tensor_tensor(eq8[:, k, :, :], eq8[:, k, :, :], bc(w2[:, :, k], NE), ALU.mult)
                link(last)
                nc.vector.tensor_tensor(comb[:, t0:t0 + RB, :], eq8[:, 0, :, :], eq8[:, 1, :, :], ALU.add)
                link(nc.vector.tensor_tensor(scomb[:, t0:t0 + RB], w2[:, :, 0], w2[:, :, 1], ALU.add))
                for t in range(t0, t0 + RB):
                    last = nc.vector.scalar_tensor_tensor(x1[:, t, :], bob_t[:, :], scomb[:, t:t + 1], x1[:, t, :],
                                                          ALU.mult, ALU.add)
                link(last)

            row_sums(0)
            normalized(0)
            dve.wait_ge(a_tanh, 1)
            dve.wait_ge(d_bout, 16)
            dve.wait_ge(d_wo, 16)
            nc.vector.tensor_scalar(wo_t[:, :].rearrange("d (c p) -> d c p", c=NC),
                                    wo[:, :].rearrange("d (p c) -> d c p", c=NC),
                                    tanh_g[:, 1:2], None, ALU.mult).then_inc(v_wo, 1)
            link(nc.vector.tensor_scalar(boutb[:, :], boutb[:, :], tanh_g[:, 0:1], None, ALU.mult))
            for i in iters:
                if i == 0:
                    link(nc.vector.tensor_tensor(x1[:, :, :], xs[:, :, :], rep(boutb[:, :], T), ALU.add))
                    dve.wait_ge(d_wout, 16)
                    nc.vector.tensor_scalar(wout_t[:, :], wout[:, :], tanh_g[:, 0:1], None, ALU.mult)
                    dve.wait_ge(d_bo, 16)
                    nc.vector.tensor_scalar(bob_t[:, :], bob[:, :], tanh_g[:, 1:2], None, ALU.mult).then_inc(v_xres, 1)
                if i == -1:
                    dve.wait_ge(s_setup, 1)
                    nc.vector.tensor_copy(woT[:, :, :], ps[:, MXB, 0:2 * P].rearrange("p (k d) -> p k d", k=2))
                    nc.vector.tensor_copy(wgT[:, :], ps[:, MXB, 2 * P:2 * P + NE]).then_inc(v_woT, 1)
                if on(i + 1):
                    maxima(i + 1, 0)
                    maxima(i + 1, 1)
                if on(i - 1):
                    t = i - 1
                    dve.wait_ge(s_OT, t + 1)
                    o = ps[:, OB, :].rearrange("p (h c) -> p h c", c=GP)
                    if t >= 2:
                        dve.wait_ge(s_aT, t - 1)
                    link(nc.vector.reciprocal(rden[:, :], o[:, :, HD]))
                    nc.vector.tensor_tensor(att[:, t % 2, :].rearrange("p (h c) -> p h c", c=HD), o[:, :, 0:HD],
                                            bc(rden[:, :], HD), ALU.mult).then_inc(v_at, 1)
                if on(i + 2):
                    t = i + 2
                    dve.wait_ge(s_AP, t + 1)
                    nc.vector.tensor_tensor(qk[:, t % 2, :, :], ps[:, AB, 0:2 * P].rearrange("p (k d) -> p k d", k=2),
                                            bc(bqk[:, 0:2], P), ALU.add).then_inc(v_qk, 1)
                    if t == 0:
                        dve.wait_ge(d_bv, 16)
                        dve.wait_ge(p_const, 5)
                    if t >= 3:
                        dve.wait_ge(s_PV, NG * (t - 2))
                    nc.vector.tensor_tensor(v_pad[:, t % 3, :, 0:HD],
                                            ps[:, AB, 2 * P:3 * P].rearrange("p (h c) -> p h c", c=HD),
                                            bvb[:, :].rearrange("p (h c two) -> p h c two", c=HD, two=2)[:, :, :, 1],
                                            ALU.add).then_inc(v_v, 1)
                if on(i + 1):
                    maxima(i + 1, 2)
                if on(i + 2):
                    t = i + 2
                    dve.wait_ge(a_hi, t + 1)
                    if t >= 3:
                        dve.wait_ge(s_SC, NG * (t - 2))
                        dve.wait_ge(p_ql, t - 2)
                    nc.vector.tensor_tensor(qk_lo[:, t % 3, :, :], qk[:, t % 2, :, :],
                                            qk_hi[:, t % 3, :, :].bitcast(fp32), ALU.subtract).then_inc(v_lo, 1)
                if on(i + 1):
                    maxima(i + 1, 3)
                if on(i - 1):
                    t = i - 1
                    dve.wait_ge(s_OP, t + 1)
                    ins = nc.vector.tensor_tensor(x1[:, t, :], ps[:, OB, 0:D], x1[:, t, :], ALU.add)
                    ins.then_inc(v_x1, 1)
                    dve.wait_ge(v_x1, t + 1)
                    link(nc.vector.bn_stats(stats2[:, t % 2, :], x1[:, t, :]))
                    link(nc.vector.bn_aggr(mv2[:, t % 2, :], stats2[:, t % 2, :]))
                    nc.vector.tensor_scalar(var2[:, t % 2:t % 2 + 1], mv2[:, t % 2, 1:2], LN_EPS, None,
                                            ALU.add).then_inc(v_var2, 1)
                if on(i + 2):
                    e = i + 2
                    dve.wait_ge(a_wh, e + 1)
                    nc.vector.tensor_tensor(w_lo[:, e, :], ps[:, WB, :], w_hi[:, e, :].bitcast(fp32),
                                            ALU.subtract).then_inc(v_wl, 1)
                if on(i + 1):
                    t = i + 1
                    dve.wait_ge(s_mT, t + 1)
                    if t >= 2:
                        dve.wait_ge(s_SC, NG * (t - 1))
                    nc.vector.tensor_tensor(max_m[:, t % 2, :, :], rep(ps[:, WB, 0:P], HG), bc(row_mask[:, :], P),
                                            ALU.mult).then_inc(v_mm, 1)
                if on(i + 3):
                    row_sums(i + 3)
                    normalized(i + 3)
                if on(i - 1):
                    t = i - 1
                    dve.wait_ge(p_rstd2, t + 1)
                    if t >= 2:
                        dve.wait_ge(s_XT, t - 1)
                    nc.vector.tensor_scalar(xn2[:, t % 2, :], x1[:, t, :], mv2[:, t % 2, 0:1],
                                            rstd2[:, t % 2:t % 2 + 1], ALU.subtract, ALU.mult).then_inc(v_xn2, 1)
                if on(i - 2):
                    t = i - 2
                    dve.wait_ge(a_xT, t + 1)
                    link(nc.vector.tensor_scalar(x_hi[:, t, :], xn2T[:, t % 2, :], 1.0, None, ALU.add))
                    nc.vector.scalar_tensor_tensor(x_lo[:, t, :], xn2T[:, t % 2, :], 1.0,
                                                   x_hi[:, t, :].bitcast(fp32), ALU.add,
                                                   ALU.subtract).then_inc(v_x2, 1)
                    if t % RB == RB - 1:
                        router(t // RB)

            def result(t):
                dve.wait_ge(s_WO, t + 1)
                if t >= 2:
                    dve.wait_ge(d_out[t % 2], 16 * (t // 2))
                nc.vector.tensor_tensor(y[:, t % 2, :], ps[:, 7, 0:D], x1[:, t, :], ALU.add).then_inc(v_y, 1)

            for t in range(T):
                for e in range(NE):
                    n = PAIRS * t + e // 2
                    if e % 2 == 0:
                        dve.wait_ge(a_sig, n + 1)
                    if e == 0:
                        dst = gacc[:, t % 2, :]
                        if t >= 2:
                            dve.wait_ge(v_gs, t - 1)
                    else:
                        dst = gl[:, e % 4, :]
                        if e == 1 and t >= 1:
                            dve.wait_ge(p_acc, (NE - 3) * t)
                        if e >= 5:
                            dve.wait_ge(p_acc, (NE - 3) * t + e - 4)
                    h4 = ps[:, 2 * (n % 3) + e % 2, :].rearrange("p (c h) -> p c h", c=NC)
                    nc.vector.scalar_tensor_tensor(
                        dst.rearrange("p (c h) -> p c h", c=NC), h4[:, :, 0:PH], comb[:, t, e:e + 1],
                        sig[:, n % 3, e % 2, :].rearrange("p (c h) -> p c h", c=NC),
                        ALU.mult, ALU.mult).then_inc(v_g, 1)
                dve.wait_ge(v_g, NE * (t + 1))
                link(nc.vector.tensor_tensor(gb[:, :], gl[:, (NE - 2) % 4, :], gl[:, (NE - 1) % 4, :], ALU.add))
                dve.wait_ge(p_acc, (NE - 3) * (t + 1))
                if t >= 2:
                    dve.wait_ge(s_GT, t - 1)
                nc.vector.tensor_tensor(gsum[:, t % 2, :], gb[:, :], gacc[:, t % 2, :], ALU.add).then_inc(v_gs, 1)
                if t >= 1:
                    result(t - 1)
            result(T - 1)

        @block.tensor
        def _(pe):
            mm = nc.tensor.matmul
            pe.wait_ge(v_wo, 1)
            pe.wait_ge(p_ident, 1)
            for k in range(2):
                nc.tensor.transpose(ps[:, MXB, k * D:(k + 1) * D], wo_t[:, k * P:(k + 1) * P], ident[:, :])
            pe.wait_ge(d_wg, 16)
            nc.tensor.transpose(ps[:, MXB, 2 * P:2 * P + NE], wg[:, :], ident[0:NE, 0:NE]).then_inc(s_setup, 1)

            def max_scores(t, g):
                n = NG * t + g
                if g == 0:
                    pe.wait_ge(p_km, t + 1)
                    if t == 0:
                        pe.wait_ge(v_ones, 2)
                        pe.wait_ge(v_woT, 1)
                if n >= 2:
                    pe.wait_ge(v_max, n - 1)
                r = slice(GP * g, GP * (g + 1))
                mm(ps[:, MXB + g % 2, :], qk_hi[r, t % 3, 0, :], k_hi_m[r, t % 2, :, :], start=True,
                   stop=True).then_inc(s_MX, 1)

            def scores(t, g):
                n = NG * t + g
                if n >= 2:
                    pe.wait_ge(a_exp, n - 1)
                if g == 0:
                    pe.wait_ge(p_ql, t + 1)
                r = slice(GP * g, GP * (g + 1))
                o = ps[:, SCB + g % 2, :]
                mm(o, qk_hi[r, t % 3, 1, :], q_hi_m[r, t % 3, :, :], start=True, stop=False)
                mm(o, qk_hi[r, t % 3, 1, :], q_lo_m[r, t % 3, :, :], start=False, stop=False)
                mm(o, qk_lo[r, t % 3, 1, :], q_hi_m[r, t % 3, :, :], start=False, stop=False)
                if g == 0:
                    pe.wait_ge(v_mm, t + 1)
                mm(o, ones_r[r, :], max_m[r, t % 2, :, :], start=False, stop=True).then_inc(s_SC, 1)

            def weighted(t, g):
                pe.wait_ge(a_exp, NG * t + g + 1)
                if g == 0 and t >= 1:
                    pe.wait_ge(a_o, t)
                for r in range(HG):
                    last = mm(ps[GP * r:GP * (r + 1), PVB, P * g:P * (g + 1)], v_pad[:, t % 3, HG * g + r, :],
                              probs[:, t % 2, g, P * r:P * (r + 1)], start=True, stop=True)
                last.then_inc(s_PV, 1)

            for i in iters:
                if on(i + 2):
                    t = i + 2
                    pe.wait_ge(v_xn, t + 1)
                    if t % (T // 2) == 0:
                        pe.wait_ge(d_c[t // (T // 2)], 16)
                    if t >= 1:
                        pe.wait_ge(v_v, t)
                    nc.tensor.transpose(ps[:, AB, 0:P], xn[:, t % 2, :], ident[:, :])
                    nc.tensor.transpose(ps[:, AB, P:2 * P], cs[:, t, :], ident[:, :]).then_inc(s_AT, 1)
                if on(i):
                    scores(i, 0)
                if on(i + 1):
                    max_scores(i + 1, 0)
                    max_scores(i + 1, 1)
                if on(i - 1):
                    t = i - 1
                    pe.wait_ge(a_o, t + 1)
                    if t >= 2:
                        pe.wait_ge(a_lg, t - 1)
                    for g in range(NG):
                        last = nc.tensor.transpose(ps[:, OB, P * g:P * (g + 1)], o_sb[:, t % 2, g, :], ident[:, :])
                    last.then_inc(s_OT, 1)
                if on(i):
                    scores(i, 1)
                    weighted(i, 0)
                if on(i + 2):
                    t = i + 2
                    pe.wait_ge(a_xc, t + 1)
                    if t == 0:
                        pe.wait_ge(v_wqk, 1)
                    xT, cT = xcT[:, t % 2, 0:P], xcT[:, t % 2, P:2 * P]
                    mm(ps[:, AB, 0:P], wqk[:, 0, :], xT, start=True, stop=True)
                    mm(ps[:, AB, P:2 * P], wqk[:, 1, :], cT, start=True, stop=True)
                    mm(ps[:, AB, 2 * P:3 * P], cT, wv[:, :], start=True, stop=True).then_inc(s_AP, 1)
                if on(i + 1):
                    max_scores(i + 1, 2)
                if on(i - 1):
                    t = i - 1
                    pe.wait_ge(v_at, t + 1)
                    nc.tensor.transpose(ps[:, OB, 0:P], att[:, t % 2, :], ident[:, :]).then_inc(s_aT, 1)
                if on(i):
                    scores(i, 2)
                    weighted(i, 1)
                if on(i + 1):
                    max_scores(i + 1, 3)
                if on(i - 1):
                    t = i - 1
                    pe.wait_ge(a_aT, t + 1)
                    if t == 0:
                        pe.wait_ge(v_xres, 1)
                    mm(ps[:, OB, 0:D], attT[:, t % 2, :], wout_t[:, :], start=True, stop=True).then_inc(s_OP, 1)
                if on(i + 2):
                    e = i + 2
                    pe.wait_ge(p_wa, e + 1)
                    if i >= 0:
                        pe.wait_ge(v_mm, i + 1)
                    for c in range(NC):
                        last = nc.tensor.transpose(ps[:, WB, P * c:P * (c + 1)], w1a[:, e % 2, D * c:D * (c + 1)],
                                                   ident[:, :])
                    last.then_inc(s_WT, 1)
                if on(i):
                    scores(i, 3)
                    weighted(i, 2)
                if on(i - 2):
                    t = i - 2
                    if on(i - 1):
                        pe.wait_ge(v_x1, i)
                    if t >= 1:
                        pe.wait_ge(a_lg, t)
                    pe.wait_ge(v_xn2, t + 1)
                    nc.tensor.transpose(ps[:, OB, 0:P], xn2[:, t % 2, :], ident[:, :]).then_inc(s_XT, 1)
                if on(i + 1):
                    t = i + 1
                    pe.wait_ge(v_max, NG * (t + 1))
                    pe.wait_ge(v_wl, min(i + 3, NE))
                    nc.tensor.transpose(ps[:, WB, 0:P], neg_max[:, t % 2, :], ident[:, :]).then_inc(s_mT, 1)
                if on(i - 2):
                    pe.wait_ge(a_xT, i - 1)
                    mm(ps[:, OB, 0:NE], xn2T[:, i % 2, :], wgT[:, :], start=True, stop=True).then_inc(s_RT, 1)
                if on(i):
                    weighted(i, 3)

            def down(t):
                pe.wait_ge(a_gT, t + 1)
                if t >= 1:
                    pe.wait_ge(v_y, t)
                for k in range(2):
                    last = mm(ps[:, 7, 0:D], gT[:, t % 2, k, :], woT[:, k, :], start=(k == 0), stop=(k == 1))
                last.then_inc(s_WO, 1)

            def turn(t):
                pe.wait_ge(v_gs, t + 1)
                if t >= 1:
                    pe.wait_ge(a_gT, t)
                for k in range(2):
                    last = nc.tensor.transpose(ps[:, 6, P * k:P * (k + 1)], gsum[:, t % 2, P * k:P * (k + 1)],
                                               ident[:, :])
                last.then_inc(s_GT, 1)

            for t in range(T):
                pe.wait_ge(v_x2, t + 1)
                for j in range(PAIRS):
                    n = PAIRS * t + j
                    if n >= 3:
                        pe.wait_ge(v_g, 2 * (n - 2))
                    for e in (2 * j, 2 * j + 1):
                        o = ps[:, 2 * (n % 3) + e % 2, :]
                        mm(o, x_hi[:, t, :], w_hi[:, e, :], start=True, stop=False)
                        mm(o, x_hi[:, t, :], w_lo[:, e, :], start=False, stop=False)
                        last = mm(o, x_lo[:, t, :], w_hi[:, e, :], start=False, stop=True)
                    last.then_inc(s_FF, 1)
                    if t >= 1 and j == 1:
                        turn(t - 1)
                    if t >= 1 and j == 2:
                        down(t - 1)
            turn(T - 1)
            down(T - 1)


_INS = ["x", "ctx_1024", "g_xattn", "g_ffn", "L0_xattn_Wq", "L0_xattn_bq", "L0_xattn_Wkv", "L0_xattn_bkv",
        "L0_xattn_Wout", "L0_xattn_bout", "L0_ffn_Wg", "L0_ffn_W1", "L0_ffn_b1", "L0_ffn_Wo", "L0_ffn_bo"]


def kernel(**inputs):
    import numpy as np
    import concourse.bacc as bacc
    from concourse.bass_utils import run_bass_kernel_spmd

    nc = bacc.Bacc("TRN2", target_bir_lowering=False, num_devices=1)
    arrays, args = {}, []
    for name in _INS:
        a = np.ascontiguousarray(inputs[name])
        arrays[f"in_{name}"] = a
        args.append(nc.dram_tensor(f"in_{name}", a.shape, mybir.dt.from_np(a.dtype), kind="ExternalInput").ap())
    shape = inputs["x"].shape
    out = nc.dram_tensor("out", shape, mybir.dt.float32, kind="ExternalOutput").ap()
    flamingo_gated_block(nc, *args, out)
    r = run_bass_kernel_spmd(nc, [arrays], core_ids=[0])
    return r.results[0]["out"]
```

```python
import concourse.bass as bass
from concourse import mybir
from contextlib import ExitStack


def flamingo_gated_block(nc, x, ctx_in, g_xattn, g_ffn, Wq, bq, Wkv, bkv, Wout, bout, Wg, W1, b1, Wo, bo, out):
    fp32, fp32r, u32 = mybir.dt.float32, mybir.dt.float32r, mybir.dt.uint32
    ALU, ACT, AX = mybir.AluOpType, mybir.ActivationFunctionType, mybir.AxisListType

    T, P, D = x.shape
    NH = 16
    HD = D // NH
    NG = 4
    HG = NH // NG
    GP = P // NG
    SCALE = float(HD) ** -0.5
    NE, H2, _ = W1.shape
    NC = H2 // P
    HH = H2 // 2
    PH = HH // NC
    LN_EPS, TOP_EPS = 1e-5, 1e-9
    T0 = 2
    RB = 4
    PAIRS = NE // 2

    es = ExitStack()
    with es:
        def sb(name, shape, dt=fp32):
            return es.enter_context(nc.sbuf_tensor(name, shape, dt))

        def sem(name):
            return es.enter_context(nc.semaphore(name))

        xs = sb("xs", [P, T, D])
        cs = sb("cs", [P, T, D])
        wq = sb("wq", [D, D])
        wkv = sb("wkv", [D, 2 * D])
        wout = sb("wout", [D, D])
        wo = sb("wo", [D, HH])
        wg = sb("wg", [NE, D])
        w1 = sb("w1", [P, NE, NC * D])
        b1s = sb("b1s", [P, NE, NC])
        bqk = sb("bqk", [D, 3])
        bvb = sb("bvb", [P, 2 * D])
        boutb = sb("boutb", [P, D])
        bob = sb("bob", [P, D])
        gates = sb("gates", [P, 2])
        ident = sb("ident", [P, P])
        head_mask = sb("head_mask", [P, HG])
        row_mask = sb("row_mask", [P, HG])
        ones_r = sb("ones_r", [P, NG, P], fp32r)
        group_mask = sb("group_mask", [P, NG])
        idle = sb("idle", [P, 512], mybir.dt.bfloat16)
        half_pow = sb("half_pow", [P, T])
        iota8 = sb("iota8", [P, NE])
        tanh_g = sb("tanh_g", [P, 2])
        wqk = sb("wqk", [D, 2, D])
        wv = sb("wv", [D, D])
        wout_t = sb("wout_t", [D, D])
        wo_t = sb("wo_t", [D, HH])
        woT = sb("woT", [P, 2, D])
        wgT = sb("wgT", [D, NE])
        bob_t = sb("bob_t", [P, D])
        stats = sb("stats", [P, T, 6])
        mv = sb("mv", [P, T, 2])
        var_eps = sb("var_eps", [P, T])
        rstd = sb("rstd", [P, T])
        xn = sb("xn", [P, 3, D])
        xcT = sb("xcT", [D, 2, 2 * P])
        qk = sb("qk", [D, 2, 2, P])
        qk_hi = sb("qk_hi", [D, 3, 2, P], fp32r)
        qk_lo = sb("qk_lo", [D, 3, 2, P], fp32r)
        q_hi_m = sb("q_hi_m", [D, 3, HG, P], fp32r)
        q_lo_m = sb("q_lo_m", [D, 3, HG, P], fp32r)
        k_hi_m = sb("k_hi_m", [D, 2, HG, P], fp32r)
        v_pad = sb("v_pad", [P, 3, NH, GP])
        neg_max = sb("neg_max", [P, 2, P])
        max_m = sb("max_m", [P, 2, HG, P], fp32r)
        probs = sb("probs", [P, 2, NG, HG * P])
        o_sb = sb("o_sb", [P, 2, NG, P])
        rden = sb("rden", [P, NH])
        att = sb("att", [P, 2, D])
        attT = sb("attT", [D, 2, P])
        x1 = sb("x1", [P, T, D])
        stats2 = sb("stats2", [P, 2, 6])
        mv2 = sb("mv2", [P, 2, 2])
        var2 = sb("var2", [P, 2])
        rstd2 = sb("rstd2", [P, 2])
        xn2 = sb("xn2", [P, 2, D])
        xn2T = sb("xn2T", [D, 2, P])
        x_hi = sb("x_hi", [D, T, P], fp32r)
        x_lo = sb("x_lo", [D, T, P], fp32r)
        lg = sb("lg", [P, T, NE])
        lmax = sb("lmax", [P, RB])
        lsub = sb("lsub", [P, RB, NE])
        pe8 = sb("pe8", [P, RB, NE])
        psum8 = sb("psum8", [P, RB])
        prec8 = sb("prec8", [P, RB])
        pr8 = sb("pr8", [P, RB, NE])
        top8 = sb("top8", [P, RB, 8])
        idx8 = sb("idx8", [P, RB, 8], u32)
        idxf = sb("idxf", [P, RB, 2])
        s2 = sb("s2", [P, RB])
        r2 = sb("r2", [P, RB])
        w2 = sb("w2", [P, RB, 2])
        eq8 = sb("eq8", [P, 2, RB, NE])
        comb = sb("comb", [P, T, NE])
        scomb = sb("scomb", [P, T])
        wsum = sb("wsum", [P, NE, NC])
        w_copy = sb("w_copy", [P, D])
        w1b = sb("w1b", [P, NE, NC])
        w_hi = sb("w_hi", [D, NE, H2], fp32r)
        w_lo = sb("w_lo", [D, NE, H2], fp32r)
        sig = sb("sig", [P, 3, 2, HH])
        gl = sb("gl", [P, 4, HH])
        gacc = sb("gacc", [P, 2, HH])
        gsum = sb("gsum", [P, 2, HH])
        gb = sb("gb", [P, HH])
        gT = sb("gT", [P, 2, 2, P])
        y = sb("y", [P, 2, D])

        ps = es.enter_context(nc.psum_tensor("ps", [P, 8, 512], fp32))
        MXB, SCB, PVB, AB, WB, OB = 0, 2, 4, 5, 6, 7

        d_x = [sem(f"d_x{n}") for n in range(2)]
        d_c = [sem(f"d_c{n}") for n in range(2)]
        d_w1 = [sem(f"d_w1_{n}") for n in range(4)]
        d_out = [sem(f"d_out{n}") for n in range(2)]
        d_g, d_wq, d_wkv, d_bqk, d_bv, d_bout, d_wout, d_wo, d_wg, d_bo, d_b1 = [
            sem(n) for n in ("d_g", "d_wq", "d_wkv", "d_bqk", "d_bv", "d_bout", "d_wout", "d_wo", "d_wg", "d_bo",
                             "d_b1")]
        (s_setup, s_AT, s_AP, s_MX, s_mT, s_SC, s_PV, s_OT, s_aT, s_OP, s_XT, s_RT, s_WT, s_FF, s_GT, s_WO) = [
            sem(n) for n in ("s_setup", "s_AT", "s_AP", "s_MX", "s_mT", "s_SC", "s_PV", "s_OT", "s_aT", "s_OP",
                             "s_XT", "s_RT", "s_WT", "s_FF", "s_GT", "s_WO")]
        (a_tanh, a_setup, a_xc, a_hi, a_exp, a_o, a_aT, a_xT, a_lg, a_re, a_wh, a_sum, a_sig, a_gT) = [
            sem(n) for n in ("a_tanh", "a_setup", "a_xc", "a_hi", "a_exp", "a_o", "a_aT", "a_xT", "a_lg", "a_re",
                             "a_wh", "a_sum", "a_sig", "a_gT")]
        (v_chain, v_masks, v_idle, v_wqk, v_var, v_xres, v_xn, v_qk, v_v, v_lo, v_max, v_mm, v_at, v_x1, v_var2, v_xn2,
         v_x2, v_sub, v_comb, v_b1, v_wo, v_wl, v_woT, v_ones, v_g, v_gs, v_y) = [
            sem(n) for n in ("v_chain", "v_masks", "v_idle", "v_wqk", "v_var", "v_xres", "v_xn", "v_qk", "v_v", "v_lo",
                             "v_max", "v_mm", "v_at", "v_x1", "v_var2", "v_xn2", "v_x2", "v_sub", "v_comb",
                             "v_b1", "v_wo", "v_wl", "v_woT", "v_ones", "v_g", "v_gs", "v_y")]
        (p_zero, p_ident, p_const, p_iota, p_rstd, p_km, p_qh, p_ql, p_rstd2, p_wa, p_acc) = [
            sem(n) for n in ("p_zero", "p_ident", "p_const", "p_iota", "p_rstd", "p_km", "p_qh", "p_ql", "p_rstd2", "p_wa",
                             "p_acc")]

        block = es.enter_context(nc.Block())

        def bc(ap, n):
            return ap.unsqueeze(2).to_broadcast([ap.shape[0], ap.shape[1], n])

        def rep(ap, n):
            return ap.unsqueeze(1).to_broadcast([ap.shape[0], n, ap.shape[1]])

        def on(t):
            return 0 <= t < T

        BUSY = (5, 2, 5, 2, 3, 3, 5, 5, 5)
        steps = range(-2, T + 2)

        @block.sync
        def _(sp):
            xt = x.rearrange("t p d -> p t d")
            w1t = W1.rearrange("e (p c) d -> p e (c d)", c=NC)
            sp.dma_start(xs[:, 0:T0], xt[:, 0:T0]).then_inc(d_x[0], 16)
            sp.dma_start(wq[:, :], Wq).then_inc(d_wq, 16)
            sp.dma_start(bvb[:, :], bkv.partition_broadcast(P)).then_inc(d_bv, 16)
            sp.dma_start(w1[:, 0:2, :], w1t[:, 0:2, :]).then_inc(d_w1[0], 16)
            sp.dma_start(xs[:, T0:T], xt[:, T0:T]).then_inc(d_x[1], 16)
            sp.dma_start(wg[:, :], Wg).then_inc(d_wg, 16)
            for n in range(1, 4):
                sp.dma_start(w1[:, 2 * n:2 * n + 2, :], w1t[:, 2 * n:2 * n + 2, :]).then_inc(d_w1[n], 16)
            sp.dma_start(boutb[:, :], bout.partition_broadcast(P)).then_inc(d_bout, 16)
            sp.dma_start(wout[:, :], Wout).then_inc(d_wout, 16)
            sp.dma_start(bob[:, :], bo.partition_broadcast(P)).then_inc(d_bo, 16)
            for t in range(T):
                sp.wait_ge(v_y, t + 1)
                sp.dma_start(out[t], y[:, t % 2, :]).then_inc(d_out[t % 2], 16)
            for n in range(2):
                sp.wait_ge(d_out[n], 16 * (T // 2))

        @block.gpsimd
        def _(pool):
            nc.gpsimd.memset(ident[:, :], 0.0).then_inc(p_zero, 1)
            pool.dma_start(gates[:, 0:1], g_xattn.partition_broadcast(P)).then_inc(d_g, 16)
            pool.dma_start(gates[:, 1:2], g_ffn.partition_broadcast(P)).then_inc(d_g, 16)
            pool.wait_ge(p_zero, 1)
            nc.gpsimd.affine_select(out=ident[:, :], in_=ident[:, :], compare_op=ALU.not_equal, fill=1.0, base=0,
                                    pattern=[[-1, P]], channel_multiplier=1).then_inc(p_ident, 1)
            nc.gpsimd.memset(half_pow[:, :], -0.5).then_inc(p_const, 1)
            pool.wait_ge(v_var, 1)
            pool.wait_ge(p_const, 1)
            nc.gpsimd.tensor_tensor(rstd[:, 0:T0], var_eps[:, 0:T0], half_pow[:, 0:T0], ALU.pow).then_inc(p_rstd, 1)
            nc.gpsimd.memset(v_pad[:, 0], 0.0).then_inc(p_const, 1)
            nc.gpsimd.memset(v_pad[:, 1:3], 0.0).then_inc(p_const, 1)
            nc.gpsimd.memset(neg_max[:, :, :], 0.0).then_inc(p_const, 1)
            pool.wait_ge(p_const, 4)
            nc.gpsimd.memset(v_pad[:, :, :, HD:HD + 1], 1.0).then_inc(p_const, 1)
            for e in range(NE):
                nc.gpsimd.memset(iota8[:, e:e + 1], float(e)).then_inc(p_iota, 1)
            def biased_w1(e):
                pool.wait_ge(v_b1, e + 1)
                w = w1[:, e, :].rearrange("p (c d) -> p c d", c=NC)
                nc.gpsimd.tensor_tensor(w, w, bc(w1b[:, e, :], D), ALU.add).then_inc(p_wa, 1)

            def masked(t):
                hm = bc(head_mask[:, :], P)
                if t == 0:
                    pool.wait_ge(v_masks, 1)
                pool.wait_ge(a_hi, t + 1)
                if t >= 2:
                    pool.wait_ge(s_MX, NG * (t - 1))
                nc.gpsimd.tensor_tensor(k_hi_m[:, t % 2], rep(qk_hi[:, t % 3, 1, :].bitcast(fp32), HG), hm,
                                        ALU.mult).then_inc(p_km, 1)
                if t >= 3:
                    pool.wait_ge(s_SC, NG * (t - 2))
                nc.gpsimd.tensor_tensor(q_hi_m[:, t % 3], rep(qk_hi[:, t % 3, 0, :].bitcast(fp32), HG), hm,
                                        ALU.mult).then_inc(p_qh, 1)
                if t == 0:
                    pool.wait_ge(v_var, 2)
                    nc.gpsimd.tensor_tensor(rstd[:, T0:T], var_eps[:, T0:T], half_pow[:, T0:T],
                                            ALU.pow).then_inc(p_rstd, 1)
                pool.wait_ge(v_lo, t + 1)
                nc.gpsimd.tensor_tensor(q_lo_m[:, t % 3], rep(qk_lo[:, t % 3, 0, :].bitcast(fp32), HG), hm,
                                        ALU.mult).then_inc(p_ql, 1)

            for i in steps:
                if on(i + 2):
                    masked(i + 2)
                if on(i + 2):
                    biased_w1(i + 2)
                if on(i - 1):
                    t = i - 1
                    pool.wait_ge(v_var2, t + 1)
                    nc.gpsimd.tensor_tensor(rstd2[:, t % 2:t % 2 + 1], var2[:, t % 2:t % 2 + 1],
                                            half_pow[:, 0:1], ALU.pow).then_inc(p_rstd2, 1)
            for t in range(T):
                for e in range(1, NE - 2):
                    pool.wait_ge(v_g, NE * t + e + 1)
                    if e > 1:
                        pool.wait_ge(p_acc, (NE - 3) * t + e - 1)
                    nc.gpsimd.tensor_tensor(gacc[:, t % 2, :], gacc[:, t % 2, :], gl[:, e % 4, :],
                                            ALU.add).then_inc(p_acc, 1)

        @block.scalar
        def _(act):
            ct = ctx_in.rearrange("t p d -> p t d")
            act.dma_start(cs[:, 0:T0], ct[:, 0:T0]).then_inc(d_c[0], 16)
            act.dma_start(wkv[:, :], Wkv).then_inc(d_wkv, 16)
            act.dma_start(bqk[:, 0:1], bq.unsqueeze(1)).then_inc(d_bqk, 16)
            act.dma_start(bqk[:, 1:3], bkv.rearrange("(d two) -> d two", two=2)).then_inc(d_bqk, 16)
            act.dma_start(wo[:, :], Wo).then_inc(d_wo, 16)
            act.dma_start(b1s[:, :, :], b1.rearrange("e (p c) -> p e c", c=NC)).then_inc(d_b1, 16)
            act.dma_start(cs[:, T0:T], ct[:, T0:T]).then_inc(d_c[1], 16)

            def row_sum(e, c):
                if c == 0:
                    act.wait_ge(d_w1[e // 2], 16)
                if e >= 1 or c >= 1:
                    act.wait_ge(a_sum, NC * e + c)
                nc.scalar.activation(w_copy[:, :], w1[:, e, D * c:D * (c + 1)], ACT.Copy,
                                     accum_out=wsum[:, e, c:c + 1]).then_inc(a_sum, 1)

            def exp(t, g):
                act.wait_ge(s_SC, NG * t + g + 1)
                if t >= 2:
                    act.wait_ge(s_PV, NG * (t - 2) + g + 1)
                nc.scalar.activation(probs[:, t % 2, g, :], ps[:, SCB + g % 2, :], ACT.Exp).then_inc(a_exp, 1)

            for i in steps:
                if on(i + 2):
                    t = i + 2
                    act.wait_ge(s_AT, t + 1)
                    if t >= 2:
                        act.wait_ge(s_AP, t - 1)
                    nc.scalar.copy(xcT[:, t % 2, :], ps[:, AB, 0:2 * P]).then_inc(a_xc, 1)
                if on(i):
                    exp(i, 0)
                    exp(i, 1)
                if i > -2 and on(i + 3):
                    row_sum(i + 3, 0)
                if on(i + 2):
                    act.wait_ge(v_qk, t + 1)
                    if t >= 3:
                        act.wait_ge(s_SC, NG * (t - 2))
                        act.wait_ge(p_ql, t - 2)
                    nc.scalar.copy(qk_hi[:, t % 3, :, :], qk[:, t % 2, :, :]).then_inc(a_hi, 1)
                if i > -2 and on(i + 3):
                    row_sum(i + 3, 1)
                if on(i - 1):
                    t = i - 1
                    act.wait_ge(s_aT, t + 1)
                    if t >= 2:
                        act.wait_ge(s_OP, t - 1)
                    nc.scalar.copy(attT[:, t % 2, :], ps[:, OB, 0:P]).then_inc(a_aT, 1)
                if on(i):
                    exp(i, 2)
                if i > -2 and on(i + 3):
                    row_sum(i + 3, 2)
                if on(i + 1):
                    act.wait_ge(s_WT, i + 2)
                    nc.scalar.copy(w_hi[:, i + 1, :], ps[:, WB, :]).then_inc(a_wh, 1)
                if i > -2 and on(i + 3):
                    row_sum(i + 3, 3)
                if on(i):
                    exp(i, 3)
                if i == -2:
                    act.wait_ge(d_g, 32)
                    nc.scalar.activation(tanh_g[:, :], gates[:, :], ACT.Tanh).then_inc(a_tanh, 1)
                    for c in range(NC):
                        row_sum(0, c)
                    for c in range(NC):
                        row_sum(1, c)
                if on(i - 2):
                    t = i - 2
                    act.wait_ge(s_XT, t + 1)
                    if t >= 2:
                        act.wait_ge(s_RT, t - 1)
                        act.wait_ge(v_x2, t - 1)
                    nc.scalar.copy(xn2T[:, t % 2, :], ps[:, OB, 0:P]).then_inc(a_xT, 1)
                    act.wait_ge(s_RT, t + 1)
                    nc.scalar.copy(lg[:, t, :], ps[:, OB, 0:NE]).then_inc(a_lg, 1)
                    if t % RB == RB - 1:
                        b = t // RB
                        act.wait_ge(v_sub, b + 1)
                        nc.scalar.activation(pe8[:, :, :], lsub[:, :, :], ACT.Exp).then_inc(a_re, 1)
                if on(i):
                    act.wait_ge(s_PV, NG * (i + 1))
                    if i >= 2:
                        act.wait_ge(s_OT, i - 1)
                    nc.scalar.copy(o_sb[:, i % 2, :, :], ps[:, PVB, :]).then_inc(a_o, 1)

            def hidden_out(t):
                act.wait_ge(s_GT, t + 1)
                if t >= 2:
                    act.wait_ge(s_WO, t - 1)
                nc.scalar.copy(gT[:, t % 2, :, :], ps[:, 6, 0:2 * P]).then_inc(a_gT, 1)

            for t in range(T):
                for j in range(PAIRS):
                    n = PAIRS * t + j
                    act.wait_ge(s_FF, n + 1)
                    if n >= 3:
                        act.wait_ge(v_g, 2 * (n - 2))
                    b = 2 * (n % 3)
                    nc.scalar.activation(
                        sig[:, n % 3, :, :].rearrange("p e (c h) -> p e c h", c=NC),
                        ps[:, b:b + 2, :].rearrange("p e (c h) -> p e c h", c=NC)[:, :, :, PH:P],
                        ACT.Sigmoid).then_inc(a_sig, 1)
                    if j == 1 and t >= 1:
                        hidden_out(t - 1)
            hidden_out(T - 1)

        @block.vector
        def _(dve):
            chain = [0]

            def link(ins):
                chain[0] += 1
                ins.then_inc(v_chain, 1)
                dve.wait_ge(v_chain, chain[0])

            def statistics(n, tiles):
                dve.wait_ge(d_x[n], 16)
                for t in tiles:
                    last = nc.vector.bn_stats(stats[:, t, :], xs[:, t, :])
                link(last)
                for t in tiles:
                    last = nc.vector.bn_aggr(mv[:, t, :], stats[:, t, :])
                link(last)
                nc.vector.tensor_scalar(var_eps[:, tiles[0]:tiles[-1] + 1], mv[:, tiles[0]:tiles[-1] + 1, 1],
                                        LN_EPS, None, ALU.add).then_inc(v_var, 1)

            nc.vector.memset(idle[:, :], 0.0).then_inc(v_idle, 1)
            statistics(0, range(0, T0))
            dve.wait_ge(p_ident, 1)
            nc.vector.tensor_reduce(head_mask[:, :], ident[:, :].rearrange("p (g r d) -> p r g d", g=NG, r=HG),
                                    AX.XY, ALU.add)
            nc.vector.tensor_reduce(row_mask[:, :], ident[:, :].rearrange("p (g c) -> p c g", g=NG)[:, 0:HG, :],
                                    AX.X, ALU.add).then_inc(v_masks, 1)
            link(nc.vector.tensor_reduce(group_mask[:, :], ident[:, :].rearrange("p (g c) -> p g c", g=NG),
                                         AX.X, ALU.add))
            nc.vector.tensor_copy(ones_r[:, :, :], bc(group_mask[:, :], P)).then_inc(v_ones, 1)
            def bias_shares(e):
                dve.wait_ge(a_sum, NC * (e + 1))
                if e == 0:
                    dve.wait_ge(d_b1, 16)
                link(nc.vector.tensor_tensor(w1b[:, e, :], b1s[:, e, :], wsum[:, e, :], ALU.subtract))
                nc.vector.tensor_scalar(w1b[:, e, :], w1b[:, e, :], 1.0 / D, None, ALU.mult).then_inc(v_b1, 1)

            def normalized(t):
                if t in (0, T0):
                    dve.wait_ge(p_rstd, 1 + (t == T0))
                if t >= 3:
                    dve.wait_ge(s_AT, t - 2)
                nc.vector.tensor_scalar(xn[:, t % 3, :], xs[:, t, :], mv[:, t, 0:1], rstd[:, t:t + 1],
                                        ALU.subtract, ALU.mult).then_inc(v_xn, 1)

            def maxima(t, g):
                dve.wait_ge(s_MX, NG * t + g + 1)
                if g == 0 and t >= 2:
                    dve.wait_ge(s_mT, t - 1)
                if g == 0 and t == 0:
                    dve.wait_ge(p_const, 4)
                nc.vector.tensor_reduce(neg_max[:, t % 2, GP * g:GP * g + HG],
                                        ps[:, MXB + g % 2, :].rearrange("p (r j) -> p r j", r=HG),
                                        AX.X, ALU.max, negate=True).then_inc(v_max, 1)

            def router(b):
                t0 = RB * b
                L = lg[:, t0:t0 + RB, :]
                dve.wait_ge(a_lg, t0 + RB)
                link(nc.vector.tensor_reduce(lmax[:, :], L, AX.X, ALU.max))
                if b:
                    dve.wait_ge(a_re, b)
                nc.vector.tensor_tensor(lsub[:, :, :], L, bc(lmax[:, :], NE), ALU.subtract).then_inc(v_sub, 1)
                dve.wait_ge(a_re, b + 1)
                link(nc.vector.tensor_reduce(psum8[:, :], pe8[:, :, :], AX.X, ALU.add))
                link(nc.vector.reciprocal(prec8[:, :], psum8[:, :]))
                link(nc.vector.tensor_tensor(pr8[:, :, :], pe8[:, :, :], bc(prec8[:, :], NE), ALU.mult))
                for k in range(RB):
                    last = nc.vector.max(top8[:, k, :], pr8[:, k, :])
                link(last)
                for k in range(RB):
                    last = nc.vector.max_index(idx8[:, k, :], top8[:, k, :], pr8[:, k, :])
                nc.vector.tensor_tensor(s2[:, :], top8[:, :, 0], top8[:, :, 1], ALU.add)
                link(last)
                if b == 0:
                    dve.wait_ge(p_iota, NE)
                link(nc.vector.tensor_copy(idxf[:, :, :], idx8[:, :, 0:2]))
                link(nc.vector.tensor_scalar(s2[:, :], s2[:, :], TOP_EPS, None, ALU.add))
                link(nc.vector.reciprocal(r2[:, :], s2[:, :]))
                link(nc.vector.tensor_tensor(w2[:, :, :], top8[:, :, 0:2], bc(r2[:, :], 2), ALU.mult))
                for k in range(2):
                    last = nc.vector.tensor_tensor(eq8[:, k, :, :], rep(iota8[:, :], RB), bc(idxf[:, :, k], NE),
                                                   ALU.is_equal)
                link(last)
                for k in range(2):
                    last = nc.vector.tensor_tensor(eq8[:, k, :, :], eq8[:, k, :, :], bc(w2[:, :, k], NE), ALU.mult)
                link(last)
                nc.vector.tensor_tensor(comb[:, t0:t0 + RB, :], eq8[:, 0, :, :], eq8[:, 1, :, :], ALU.add)
                link(nc.vector.tensor_tensor(scomb[:, t0:t0 + RB], w2[:, :, 0], w2[:, :, 1], ALU.add))
                for t in range(t0, t0 + RB):
                    last = nc.vector.scalar_tensor_tensor(x1[:, t, :], bob_t[:, :], scomb[:, t:t + 1], x1[:, t, :],
                                                          ALU.mult, ALU.add)
                link(last)

            normalized(0)
            normalized(1)
            dve.wait_ge(d_wq, 16)
            nc.vector.tensor_scalar(wqk[:, 0, :], wq[:, :], SCALE, None, ALU.mult)
            dve.wait_ge(d_wkv, 16)
            kv = wkv[:, :].rearrange("p (d two) -> p two d", two=2)
            nc.vector.tensor_copy(wqk[:, 1, :], kv[:, 0, :])
            nc.vector.tensor_copy(wv[:, :], kv[:, 1, :]).then_inc(v_wqk, 1)
            dve.wait_ge(d_bqk, 32)
            link(nc.vector.tensor_scalar(bqk[:, 0:1], bqk[:, 0:1], SCALE, None, ALU.mult))

            for i in steps:
                if i == 0:
                    dve.wait_ge(a_tanh, 1)
                    dve.wait_ge(d_bout, 16)
                    link(nc.vector.tensor_scalar(boutb[:, :], boutb[:, :], tanh_g[:, 0:1], None, ALU.mult))
                    link(nc.vector.tensor_tensor(x1[:, :, :], xs[:, :, :], rep(boutb[:, :], T), ALU.add))
                    dve.wait_ge(d_wout, 16)
                    nc.vector.tensor_scalar(wout_t[:, :], wout[:, :], tanh_g[:, 0:1], None, ALU.mult)
                    dve.wait_ge(d_bo, 16)
                    nc.vector.tensor_scalar(bob_t[:, :], bob[:, :], tanh_g[:, 1:2], None, ALU.mult).then_inc(v_xres, 1)
                    dve.wait_ge(d_wo, 16)
                    nc.vector.tensor_scalar(wo_t[:, :].rearrange("d (c p) -> d c p", c=NC),
                                            wo[:, :].rearrange("d (p c) -> d c p", c=NC),
                                            tanh_g[:, 1:2], None, ALU.mult).then_inc(v_wo, 1)
                if i == 1:
                    dve.wait_ge(s_setup, 1)
                    nc.vector.tensor_copy(woT[:, :, :], ps[:, OB, 0:2 * P].rearrange("p (k d) -> p k d", k=2))
                    nc.vector.tensor_copy(wgT[:, :], ps[:, OB, 2 * P:2 * P + NE]).then_inc(v_woT, 1)
                if on(i + 1):
                    maxima(i + 1, 0)
                    maxima(i + 1, 1)
                if i == -1:
                    normalized(2)
                if on(i - 1):
                    t = i - 1
                    dve.wait_ge(s_OT, t + 1)
                    o = ps[:, OB, :].rearrange("p (h c) -> p h c", c=GP)
                    if t >= 2:
                        dve.wait_ge(s_aT, t - 1)
                    link(nc.vector.reciprocal(rden[:, :], o[:, :, HD]))
                    nc.vector.tensor_tensor(att[:, t % 2, :].rearrange("p (h c) -> p h c", c=HD), o[:, :, 0:HD],
                                            bc(rden[:, :], HD), ALU.mult).then_inc(v_at, 1)
                if on(i + 2):
                    t = i + 2
                    dve.wait_ge(s_AP, t + 1)
                    nc.vector.tensor_tensor(qk[:, t % 2, :, :], ps[:, AB, 0:2 * P].rearrange("p (k d) -> p k d", k=2),
                                            bc(bqk[:, 0:2], P), ALU.add).then_inc(v_qk, 1)
                    if t == 0:
                        dve.wait_ge(d_bv, 16)
                        dve.wait_ge(p_const, 5)
                    if t >= 3:
                        dve.wait_ge(s_PV, NG * (t - 2))
                    nc.vector.tensor_tensor(v_pad[:, t % 3, :, 0:HD],
                                            ps[:, AB, 2 * P:3 * P].rearrange("p (h c) -> p h c", c=HD),
                                            bvb[:, :].rearrange("p (h c two) -> p h c two", c=HD, two=2)[:, :, :, 1],
                                            ALU.add).then_inc(v_v, 1)
                if on(i + 1):
                    maxima(i + 1, 2)
                if on(i + 2):
                    t = i + 2
                    dve.wait_ge(a_hi, t + 1)
                    if t >= 3:
                        dve.wait_ge(s_SC, NG * (t - 2))
                        dve.wait_ge(p_ql, t - 2)
                    nc.vector.tensor_tensor(qk_lo[:, t % 3, :, :], qk[:, t % 2, :, :],
                                            qk_hi[:, t % 3, :, :].bitcast(fp32), ALU.subtract).then_inc(v_lo, 1)
                if i == -2:
                    statistics(1, range(T0, T))
                if on(i + 2):
                    bias_shares(i + 2)
                if on(i + 1):
                    maxima(i + 1, 3)
                if on(i - 1):
                    t = i - 1
                    dve.wait_ge(s_OP, t + 1)
                    ins = nc.vector.tensor_tensor(x1[:, t, :], ps[:, OB, 0:D], x1[:, t, :], ALU.add)
                    ins.then_inc(v_x1, 1)
                    dve.wait_ge(v_x1, t + 1)
                    link(nc.vector.bn_stats(stats2[:, t % 2, :], x1[:, t, :]))
                    link(nc.vector.bn_aggr(mv2[:, t % 2, :], stats2[:, t % 2, :]))
                    nc.vector.tensor_scalar(var2[:, t % 2:t % 2 + 1], mv2[:, t % 2, 1:2], LN_EPS, None,
                                            ALU.add).then_inc(v_var2, 1)
                if on(i + 1):
                    dve.wait_ge(a_wh, i + 2)
                    nc.vector.tensor_tensor(w_lo[:, i + 1, :], ps[:, WB, :], w_hi[:, i + 1, :].bitcast(fp32),
                                            ALU.subtract).then_inc(v_wl, 1)
                if on(i + 1):
                    t = i + 1
                    dve.wait_ge(s_mT, t + 1)
                    if t >= 2:
                        dve.wait_ge(s_SC, NG * (t - 1))
                    nc.vector.tensor_tensor(max_m[:, t % 2, :, :], rep(ps[:, WB, 0:P], HG), bc(row_mask[:, :], P),
                                            ALU.mult).then_inc(v_mm, 1)
                if on(i + 4) and i > -2:
                    normalized(i + 4)
                if on(i - 1):
                    t = i - 1
                    dve.wait_ge(p_rstd2, t + 1)
                    if t >= 2:
                        dve.wait_ge(s_XT, t - 1)
                    nc.vector.tensor_scalar(xn2[:, t % 2, :], x1[:, t, :], mv2[:, t % 2, 0:1],
                                            rstd2[:, t % 2:t % 2 + 1], ALU.subtract, ALU.mult).then_inc(v_xn2, 1)
                if on(i - 2):
                    t = i - 2
                    dve.wait_ge(a_xT, t + 1)
                    link(nc.vector.tensor_scalar(x_hi[:, t, :], xn2T[:, t % 2, :], 1.0, None, ALU.add))
                    nc.vector.scalar_tensor_tensor(x_lo[:, t, :], xn2T[:, t % 2, :], 1.0,
                                                   x_hi[:, t, :].bitcast(fp32), ALU.add,
                                                   ALU.subtract).then_inc(v_x2, 1)
                    if t % RB == RB - 1:
                        router(t // RB)

            def result(t):
                dve.wait_ge(s_WO, t + 1)
                if t >= 2:
                    dve.wait_ge(d_out[t % 2], 16 * (t // 2))
                nc.vector.tensor_tensor(y[:, t % 2, :], ps[:, 7, 0:D], x1[:, t, :], ALU.add).then_inc(v_y, 1)

            for t in range(T):
                for e in range(NE):
                    n = PAIRS * t + e // 2
                    if e % 2 == 0:
                        dve.wait_ge(a_sig, n + 1)
                    if e == 0:
                        dst = gacc[:, t % 2, :]
                        if t >= 2:
                            dve.wait_ge(v_gs, t - 1)
                    else:
                        dst = gl[:, e % 4, :]
                        if e == 1 and t >= 1:
                            dve.wait_ge(p_acc, (NE - 3) * t)
                        if e >= 5:
                            dve.wait_ge(p_acc, (NE - 3) * t + e - 4)
                    h4 = ps[:, 2 * (n % 3) + e % 2, :].rearrange("p (c h) -> p c h", c=NC)
                    nc.vector.scalar_tensor_tensor(
                        dst.rearrange("p (c h) -> p c h", c=NC), h4[:, :, 0:PH], comb[:, t, e:e + 1],
                        sig[:, n % 3, e % 2, :].rearrange("p (c h) -> p c h", c=NC),
                        ALU.mult, ALU.mult).then_inc(v_g, 1)
                dve.wait_ge(v_g, NE * (t + 1))
                link(nc.vector.tensor_tensor(gb[:, :], gl[:, (NE - 2) % 4, :], gl[:, (NE - 1) % 4, :], ALU.add))
                dve.wait_ge(p_acc, (NE - 3) * (t + 1))
                if t >= 2:
                    dve.wait_ge(s_GT, t - 1)
                nc.vector.tensor_tensor(gsum[:, t % 2, :], gb[:, :], gacc[:, t % 2, :], ALU.add).then_inc(v_gs, 1)
                if t >= 1:
                    result(t - 1)
            result(T - 1)

        @block.tensor
        def _(pe):
            mm = nc.tensor.matmul
            def max_scores(t, g):
                n = NG * t + g
                if g == 0:
                    pe.wait_ge(p_km, t + 1)
                    if t == 0:
                        pe.wait_ge(v_ones, 1)
                if n >= 2:
                    pe.wait_ge(v_max, n - 1)
                r = slice(GP * g, GP * (g + 1))
                mm(ps[:, MXB + g % 2, :], qk_hi[r, t % 3, 0, :], k_hi_m[r, t % 2, :, :], start=True,
                   stop=True).then_inc(s_MX, 1)

            def scores(t, g):
                n = NG * t + g
                if n >= 2:
                    pe.wait_ge(a_exp, n - 1)
                if g == 0:
                    pe.wait_ge(p_ql, t + 1)
                r = slice(GP * g, GP * (g + 1))
                o = ps[:, SCB + g % 2, :]
                mm(o, qk_hi[r, t % 3, 1, :], q_hi_m[r, t % 3, :, :], start=True, stop=False)
                mm(o, qk_hi[r, t % 3, 1, :], q_lo_m[r, t % 3, :, :], start=False, stop=False)
                mm(o, qk_lo[r, t % 3, 1, :], q_hi_m[r, t % 3, :, :], start=False, stop=False)
                if g == 0:
                    pe.wait_ge(v_mm, t + 1)
                mm(o, ones_r[:, g, :], max_m[:, t % 2, :, :], start=False, stop=True).then_inc(s_SC, 1)

            def weighted(t, g):
                pe.wait_ge(a_exp, NG * t + g + 1)
                if g == 0 and t >= 1:
                    pe.wait_ge(a_o, t)
                for r in range(HG):
                    last = mm(ps[GP * r:GP * (r + 1), PVB, P * g:P * (g + 1)], v_pad[:, t % 3, HG * g + r, :],
                              probs[:, t % 2, g, P * r:P * (r + 1)], start=True, stop=True)
                last.then_inc(s_PV, 1)

            def keep_busy(n):
                for _ in range(n):
                    mm(ps[:, OB, :], idle[:, 0:P], idle[:, :], start=True, stop=True)

            pe.wait_ge(v_idle, 1)
            keep_busy(BUSY[0])
            pe.wait_ge(p_ident, 1)
            for i in steps:
                if on(i + 2):
                    t = i + 2
                    pe.wait_ge(v_xn, t + 1)
                    if t in (0, T0):
                        pe.wait_ge(d_c[t == T0], 16)
                    if t >= 1:
                        pe.wait_ge(v_v, t)
                    nc.tensor.transpose(ps[:, AB, 0:P], xn[:, t % 3, :], ident[:, :])
                    nc.tensor.transpose(ps[:, AB, P:2 * P], cs[:, t, :], ident[:, :]).then_inc(s_AT, 1)
                    if t < 2:
                        keep_busy(BUSY[1 + 2 * t])
                if on(i):
                    scores(i, 0)
                if on(i + 1):
                    max_scores(i + 1, 0)
                    max_scores(i + 1, 1)
                if i == -1:
                    keep_busy(BUSY[5])
                if on(i - 1):
                    t = i - 1
                    pe.wait_ge(a_o, t + 1)
                    if t == 0:
                        pe.wait_ge(v_woT, 1)
                    if t >= 2:
                        pe.wait_ge(a_lg, t - 1)
                    for g in range(NG):
                        last = nc.tensor.transpose(ps[:, OB, P * g:P * (g + 1)], o_sb[:, t % 2, g, :], ident[:, :])
                    last.then_inc(s_OT, 1)
                if on(i):
                    scores(i, 1)
                    weighted(i, 0)
                if on(i + 2):
                    t = i + 2
                    pe.wait_ge(a_xc, t + 1)
                    if t == 0:
                        pe.wait_ge(v_wqk, 1)
                    xT, cT = xcT[:, t % 2, 0:P], xcT[:, t % 2, P:2 * P]
                    mm(ps[:, AB, 0:P], wqk[:, 0, :], xT, start=True, stop=True)
                    mm(ps[:, AB, P:2 * P], wqk[:, 1, :], cT, start=True, stop=True)
                    mm(ps[:, AB, 2 * P:3 * P], cT, wv[:, :], start=True, stop=True).then_inc(s_AP, 1)
                    if t < 2:
                        keep_busy(BUSY[2 + 2 * t])
                if on(i + 1):
                    max_scores(i + 1, 2)
                if on(i - 1):
                    t = i - 1
                    pe.wait_ge(v_at, t + 1)
                    nc.tensor.transpose(ps[:, OB, 0:P], att[:, t % 2, :], ident[:, :]).then_inc(s_aT, 1)
                if on(i):
                    scores(i, 2)
                    weighted(i, 1)
                if on(i + 1):
                    max_scores(i + 1, 3)
                if i == -1:
                    keep_busy(BUSY[6])
                if on(i - 1):
                    t = i - 1
                    pe.wait_ge(a_aT, t + 1)
                    if t == 0:
                        pe.wait_ge(v_xres, 1)
                    mm(ps[:, OB, 0:D], attT[:, t % 2, :], wout_t[:, :], start=True, stop=True).then_inc(s_OP, 1)
                if on(i + 1):
                    pe.wait_ge(p_wa, i + 2)
                    if i >= 0:
                        pe.wait_ge(v_mm, i + 1)
                    for c in range(NC):
                        last = nc.tensor.transpose(ps[:, WB, P * c:P * (c + 1)],
                                                   w1[:, i + 1, D * c:D * (c + 1)], ident[:, :])
                    last.then_inc(s_WT, 1)
                if i == -1:
                    keep_busy(BUSY[7])
                if on(i):
                    scores(i, 3)
                    weighted(i, 2)
                if on(i - 2):
                    t = i - 2
                    if on(i - 1):
                        pe.wait_ge(v_x1, i)
                    if t >= 1:
                        pe.wait_ge(a_lg, t)
                    pe.wait_ge(v_xn2, t + 1)
                    nc.tensor.transpose(ps[:, OB, 0:P], xn2[:, t % 2, :], ident[:, :]).then_inc(s_XT, 1)
                if on(i + 1):
                    t = i + 1
                    pe.wait_ge(v_max, NG * (t + 1))
                    pe.wait_ge(v_wl, t + 1)
                    nc.tensor.transpose(ps[:, WB, 0:P], neg_max[:, t % 2, :], ident[:, :]).then_inc(s_mT, 1)
                if i == -1:
                    keep_busy(BUSY[8])
                if on(i):
                    weighted(i, 3)
                if on(i - 2):
                    pe.wait_ge(a_xT, i - 1)
                    mm(ps[:, OB, 0:NE], xn2T[:, i % 2, :], wgT[:, :], start=True, stop=True).then_inc(s_RT, 1)
                if i == 0:
                    pe.wait_ge(v_wo, 1)
                    for k in range(2):
                        nc.tensor.transpose(ps[:, OB, k * D:(k + 1) * D], wo_t[:, k * P:(k + 1) * P], ident[:, :])
                    pe.wait_ge(d_wg, 16)
                    nc.tensor.transpose(ps[:, OB, 2 * P:2 * P + NE], wg[:, :], ident[0:NE, 0:NE]).then_inc(s_setup, 1)

            def down(t):
                pe.wait_ge(a_gT, t + 1)
                if t >= 1:
                    pe.wait_ge(v_y, t)
                for k in range(2):
                    last = mm(ps[:, 7, 0:D], gT[:, t % 2, k, :], woT[:, k, :], start=(k == 0), stop=(k == 1))
                last.then_inc(s_WO, 1)

            def turn(t):
                pe.wait_ge(v_gs, t + 1)
                if t >= 1:
                    pe.wait_ge(a_gT, t)
                for k in range(2):
                    last = nc.tensor.transpose(ps[:, 6, P * k:P * (k + 1)], gsum[:, t % 2, P * k:P * (k + 1)],
                                               ident[:, :])
                last.then_inc(s_GT, 1)

            for t in range(T):
                pe.wait_ge(v_x2, t + 1)
                for j in range(PAIRS):
                    n = PAIRS * t + j
                    if n >= 3:
                        pe.wait_ge(v_g, 2 * (n - 2))
                    for e in (2 * j, 2 * j + 1):
                        o = ps[:, 2 * (n % 3) + e % 2, :]
                        mm(o, x_hi[:, t, :], w_hi[:, e, :], start=True, stop=False)
                        mm(o, x_hi[:, t, :], w_lo[:, e, :], start=False, stop=False)
                        last = mm(o, x_lo[:, t, :], w_hi[:, e, :], start=False, stop=True)
                    last.then_inc(s_FF, 1)
                    if t >= 1 and j == 1:
                        turn(t - 1)
                    if t >= 1 and j == 2:
                        down(t - 1)
            turn(T - 1)
            down(T - 1)


_INS = ["x", "ctx_1024", "g_xattn", "g_ffn", "L0_xattn_Wq", "L0_xattn_bq", "L0_xattn_Wkv", "L0_xattn_bkv",
        "L0_xattn_Wout", "L0_xattn_bout", "L0_ffn_Wg", "L0_ffn_W1", "L0_ffn_b1", "L0_ffn_Wo", "L0_ffn_bo"]


def kernel(**inputs):
    import numpy as np
    import concourse.bacc as bacc
    from concourse.bass_utils import run_bass_kernel_spmd

    nc = bacc.Bacc("TRN2", target_bir_lowering=False, num_devices=1)
    arrays, args = {}, []
    for name in _INS:
        a = np.ascontiguousarray(inputs[name])
        arrays[f"in_{name}"] = a
        args.append(nc.dram_tensor(f"in_{name}", a.shape, mybir.dt.from_np(a.dtype), kind="ExternalInput").ap())
    shape = inputs["x"].shape
    out = nc.dram_tensor("out", shape, mybir.dt.float32, kind="ExternalOutput").ap()
    flamingo_gated_block(nc, *args, out)
    r = run_bass_kernel_spmd(nc, [arrays], core_ids=[0])
    return r.results[0]["out"]
```
